# Optimizing a Trainium2 kernel written in Bass

```python
import numpy as np
import jax
import jax.numpy as jnp

def _softmax(x, axis=-1):
    return jax.nn.softmax(x, axis=axis)

def _gelu(x):
    return jax.nn.gelu(x, approximate=True)

def _silu(x):
    return jax.nn.silu(x)

def _sigmoid(x):
    return jax.nn.sigmoid(x)

def _layernorm(x, axis=-1, eps=1e-05):
    m = jnp.mean(x, axis=axis, keepdims=True)
    v = jnp.var(x, axis=axis, keepdims=True)
    return (x - m) / jnp.sqrt(v + eps)

def _scatter_add(tgt, idx, src, axis=0):
    return tgt.at[idx].add(src)

def _segment_sum(src, seg, n):
    return jax.ops.segment_sum(src, seg, n)
kernel_name = 'mk_rec_standalone_d1_rec_r8_8570af'

def setup_inputs(seed: int=0):
    np.random.seed(seed)
    _w = jnp.asarray

    def _rec_inputs():
        import jax
        import jax.numpy as jnp
        _rk = jax.random.key(seed)
        r_x = -0.000611745 + 1.00059 * jax.random.normal(jax.random.fold_in(_rk, 1), (512, 39, 32), jnp.float32)
        return r_x
    r_x = _rec_inputs()

    def _L0_rec_setup():
        import jax, jax.numpy as jnp
        import numpy as np
        LAYER_SIZE = [200, 200, 200]
        SPLIT_HALF = True
        key = jax.random.key(seed)
        ks = jax.random.split(key, 8)
        B, F0, D = (256, 39, 32)
        field_nums = [F0]
        for i, s in enumerate(LAYER_SIZE):
            field_nums.append(s // 2 if SPLIT_HALF and i != len(LAYER_SIZE) - 1 else s)
        inp = {'x': jax.random.normal(ks[0], (B, F0, D), dtype=jnp.float32)}
        for i, s in enumerate(LAYER_SIZE):
            fan_in = field_nums[i] * F0
            scale = float(np.sqrt(6.0 / (fan_in + s)))
            inp[f'W{i}'] = jax.random.uniform(ks[1 + i], (fan_in, s), dtype=jnp.float32, minval=-scale, maxval=scale)
            inp[f'b{i}'] = jnp.zeros((s,), dtype=jnp.float32)
        return inp
    _L0_rec_all = _L0_rec_setup()
    _L0_rec_in = {k: v for k, v in _L0_rec_all.items() if k in ('W0', 'W1', 'W2', 'b0', 'b1', 'b2')}
    del _L0_rec_all
    return {'r_x': r_x, 'L0_rec_W0': _L0_rec_in['W0'], 'L0_rec_W1': _L0_rec_in['W1'], 'L0_rec_W2': _L0_rec_in['W2'], 'L0_rec_b0': _L0_rec_in['b0'], 'L0_rec_b1': _L0_rec_in['b1'], 'L0_rec_b2': _L0_rec_in['b2']}

def reference(r_x, L0_rec_W0, L0_rec_W1, L0_rec_W2, L0_rec_b0, L0_rec_b1, L0_rec_b2):
    import jax
    import jax.numpy as jnp

    def _L0_rec_ref(x, W0, W1, W2, b0, b1, b2):
        import jax, jax.numpy as jnp
        import numpy as np
        LAYER_SIZE = [200, 200, 200]
        SPLIT_HALF = True
        Ws = [W0, W1, W2]
        bs = [b0, b1, b2]
        B, F0, D = x.shape
        hidden = x
        finals = []
        n_layers = len(LAYER_SIZE)
        for i in range(n_layers):
            z = jnp.einsum('bmd,bnd->bmnd', x, hidden).reshape(B, -1, D)
            cur = jnp.einsum('bcd,co->bod', z, Ws[i]) + bs[i][None, :, None]
            cur = jax.nn.relu(cur)
            if SPLIT_HALF and i != n_layers - 1:
                half = LAYER_SIZE[i] // 2
                hidden, direct = (cur[:, :half, :], cur[:, half:, :])
            else:
                direct = cur
                hidden = cur
            finals.append(direct)
        result = jnp.concatenate(finals, axis=1)
        return jnp.sum(result, axis=-1)
    y = _L0_rec_ref(r_x, L0_rec_W0, L0_rec_W1, L0_rec_W2, L0_rec_b0, L0_rec_b1, L0_rec_b2)
    return y

_drawn_inputs = setup_inputs


def setup_inputs(seed=0):
    import zlib

    import numpy as np

    out = dict(_drawn_inputs(seed))
    spreads = {'L0_rec_b0': (0.0, 0.1), 'L0_rec_b1': (0.0, 0.1), 'L0_rec_b2': (0.0, 0.1)}
    factors = {}
    for name, (base, spread) in spreads.items():
        noise = np.random.default_rng([zlib.crc32(name.encode()), seed]).standard_normal(out[name].shape)
        drawn = base * np.exp(spread * noise) if base else spread * noise
        out[name] = jnp.asarray(drawn.astype(out[name].dtype))
    for name, factor in factors.items():
        out[name] = (out[name] * factor).astype(out[name].dtype)
    return out
```

```python
from contextlib import ExitStack

import concourse.bass as bass
from concourse import mybir

F32 = mybir.dt.float32
F32R = mybir.dt.float32r
ALU = mybir.AluOpType
ACT = mybir.ActivationFunctionType

P = 128
B, F, D = 512, 39, 32
O = 200
HID = 100
T = 256
TILES = T // P
BT = T // D
BLOCKS = B * D // T
TOK = B * D

SHIFTS = 3
L0_ONES = SHIFTS * F
L0_ROWS = L0_ONES + 1
L0_PAIRS = (F + 1) // 2
L0_CHUNKS = -(-L0_PAIRS // SHIFTS)
XROWS = F + SHIFTS * L0_CHUNKS - 1

MAIN = 96
TAIL = HID - MAIN
CHUNKS = 31
GROUP = 8
GROUPS = 4
TAIL_M = 7
TAIL_CHUNKS = -(-F // TAIL_M)
ONES_ROW = MAIN + TAIL_M * TAIL
BIAS_CHUNK = GROUP * (GROUPS - 1)

BATCH = 4
L0_BATCHES = [(0, 4, False), (4, 3, False)]
L12_BATCHES = [(c, min(BATCH, CHUNKS - c), c == 0) for c in range(0, CHUNKS, BATCH)]
BATCHES = {0: L0_BATCHES, 1: L12_BATCHES, 2: L12_BATCHES}
SPLITS = {l: sum(not w for _, _, w in BATCHES[l]) for l in BATCHES}
WHOLE_CHUNKS = 4
L12_SPLIT = CHUNKS - WHOLE_CHUNKS
RING = 4
PER_BLOCK = SPLITS[0] + SPLITS[1] + SPLITS[2]
AHEAD = 6
DIRECT = {0: (HID, O), 1: (HID, O), 2: (0, O)}
OUT_AT = {0: 0, 1: HID, 2: 2 * HID}
OUT_COLS = 4 * HID


def split_number(layer, blk, k):
    if layer == 0:
        return k if isinstance(blk, int) and blk == 0 else SPLITS[0] + PER_BLOCK * (blk - 1) + SPLITS[1] + k
    if layer == 1:
        return SPLITS[0] + PER_BLOCK * blk + k
    last = isinstance(blk, int) and blk == BLOCKS - 1
    return SPLITS[0] + PER_BLOCK * blk + SPLITS[1] + (0 if last else SPLITS[0]) + k


def ring_slot(layer, blk, k):
    assert PER_BLOCK % RING == 0
    if layer == 0:
        first = 0 if isinstance(blk, int) and blk == 0 else SPLITS[0] + SPLITS[1]
        return (first + k) % RING
    if layer == 1:
        return (SPLITS[0] + k) % RING
    return split_number(2, blk if isinstance(blk, int) else 0, k) % RING


def whole_number(layer, blk):
    return 2 * blk + layer - 1


def transpose_number(layer, blk):
    return 2 * blk + layer


def order(n, more):
    turn = [(1, n, b) for b in range(AHEAD, len(L12_BATCHES))]
    if more:
        turn += [(0, n + 1, b) for b in range(len(L0_BATCHES))]
    turn += [(2, n, b) for b in range(len(L12_BATCHES))]
    if more:
        turn += [(1, n + 1, b) for b in range(AHEAD)]
    return turn


def cin_kernel(nc, r_x, W0, W1, W2, b0, b1, b2, out):
    x, w0 = r_x.tensor, W0.tensor
    xt = nc.dram_tensor("x_by_field", [XROWS, TOK], F32)
    w0c = nc.dram_tensor("w0_columns_again", [F, 2 * F, O], F32)
    w0r = nc.dram_tensor("w0_rows_again", [2 * F, F, O], F32)
    xt_t, w0c_t, w0r_t = xt.ap().tensor, w0c.ap().tensor, w0r.ap().tensor

    with ExitStack() as ctx:
        def sb(name, shape, dt=F32):
            return ctx.enter_context(nc.sbuf_tensor(name, shape, dt))

        def bank(name):
            return ctx.enter_context(nc.psum_tensor(name, [P, 512], F32))

        def sem(name):
            return ctx.enter_context(nc.semaphore(name))

        w_split = {l: sb(f"w_split{l}", [P, n, 2 * O], F32R) for l, n in ((0, L0_CHUNKS), (1, L12_SPLIT), (2, L12_SPLIT))}
        w_whole = {l: sb(f"w_whole{l}", [P, WHOLE_CHUNKS, O]) for l in (1, 2)}
        xb = sb("xb", [P, CHUNKS, T])
        staged = xb[:, :, :].rearrange("p c t -> p (c t)")
        x_left = sb("x_left", [P, T])
        x_right = sb("x_right", [P, L0_CHUNKS, T])
        hid = {1: sb("hid1", [P, GROUPS, T]), 2: sb("hid2", [P, GROUPS, T])}
        z = sb("z", [P, RING, BATCH * T])
        z_whole = sb("z_whole", [P, BATCH * T])
        z_high = [sb(f"z_high{i}", [P, BATCH * T], F32R) for i in range(RING)]
        z_low = [sb(f"z_low{i}", [P, BATCH * T], F32R) for i in range(RING)]
        s = {l: sb(f"s{l}", [P, TILES, O]) for l in range(3)}
        ident = sb("ident", [P, P])
        group_b = sb("group_b", [P, TILES, BT])
        o_row = {0: sb("o_row0", [BT, HID]), 2: sb("o_row12", [BT, OUT_COLS - HID])}

        acc = {l: [bank(f"acc{l}{t}") for t in range(TILES)] for l in range(3)}
        turned = bank("turned")
        summed = bank("summed")

        xt_done = sem("xt_done")
        w0_again = [sem("w0c_done"), sem("w0r_done")]
        pairs_in = sem("pairs_in")
        xb_in = [sem(f"xb_in{g}") for g in range(GROUPS)]
        XB_COUNT = [32] * (GROUPS - 1) + [16 + 16 * TAIL_CHUNKS]
        w_in = {l: sem(f"w_in{l}") for l in range(3)}
        w_whole_in = sem("w_whole_in")
        cleared = sem("cleared")
        wz = sem("wz")
        pair_sum = sem("pair_sum")
        w_high_done = sem("w_high_done")
        w_low_done = sem("w_low_done")
        ones_set = sem("ones_set")
        ones_l0 = sem("ones_l0")
        ones_hid = sem("ones_hid")
        consts = sem("consts")
        consts_step = sem("consts_step")
        product = sem("product")
        whole = sem("whole")
        high = sem("high")
        low = sem("low")
        slots_freed = sem("slots_freed")
        whole_used = sem("whole_used")
        tile0 = [sem(f"tile0_{l}") for l in range(3)]
        second_half = [sem(f"second_half{l}") for l in range(3)]
        s_in = [sem(f"s_in{l}") for l in range(3)]
        relu_done = [sem(f"relu{l}") for l in range(3)]
        turned_in = sem("turned_in")
        hid_in = {1: sem("hid1_in"), 2: sem("hid2_in")}
        tail_in = {1: sem("tail1_in"), 2: sem("tail2_in")}
        direct_summed = [sem(f"direct_summed{l}") for l in range(3)]
        o_in = {0: sem("o0_in"), 2: sem("o12_in")}
        o_out = {0: sem("o0_out"), 2: sem("o12_out")}

        block = ctx.enter_context(nc.Block())

        Q_AT = L12_SPLIT * O

        def stage(n):
            return staged[:, 0:n * O].rearrange("p (c o) -> p c o", o=O)

        pair_w = z[:, :, :].rearrange("p a b -> p (a b)")[:, 0:L0_CHUNKS * O].rearrange("p (c o) -> p c o", o=O)
        pair_w2 = staged[:, Q_AT:Q_AT + L0_CHUNKS * O].rearrange("p (c o) -> p c o", o=O)

        @block.sync
        def _(sp):
            def turn_x(blk):
                src = [[D, F], [F * D, BT], [1, D]]
                dst = [[TOK, F], [D, BT], [1, D]]
                n2 = XROWS - F
                sp.dma_start(bass.AP(xt_t, blk * T, dst), bass.AP(x, blk * (BT * F * D), src)).then_inc(xt_done, 16)
                sp.dma_start(bass.AP(xt_t, blk * T + F * TOK, [[TOK, n2]] + dst[1:]),
                             bass.AP(x, blk * (BT * F * D), [[D, n2]] + src[1:])).then_inc(xt_done, 16)

            def load_pairs(blk):
                for k in range(SHIFTS):
                    at = slice(k * F, (k + 1) * F)
                    sp.dma_start(x_left[at, :], bass.AP(xt_t, blk * T, [[TOK, F], [1, T]])).then_inc(pairs_in, 16)
                    sp.dma_start(x_right[at, :, :],
                                 bass.AP(xt_t, blk * T + k * TOK, [[TOK, F], [SHIFTS * TOK, L0_CHUNKS], [1, T]]))\
                      .then_inc(pairs_in, 16)

            def load_xb(blk, g):
                n = min(GROUP, CHUNKS - GROUP * g)
                sp.dma_start(xb[0:MAIN, GROUP * g:GROUP * g + n, :],
                             bass.AP(xt_t, blk * T + GROUP * g * TOK, [[0, MAIN], [TOK, n], [1, T]])).then_inc(xb_in[g], 16)
                if g < GROUPS - 1:
                    sp.dma_start(xb[MAIN:P, GROUP * g:GROUP * g + n, :],
                                 bass.AP(xt_t, blk * T + CHUNKS * TOK, [[0, P - MAIN], [TOK, n], [1, T]])).then_inc(xb_in[g], 16)
                else:
                    for i in range(TAIL_CHUNKS):
                        nj = min(TAIL_M, F - TAIL_M * i)
                        sp.dma_start(xb[MAIN:MAIN + TAIL * nj, BIAS_CHUNK + i, :],
                                     bass.AP(xt_t, blk * T + TAIL_M * i * TOK, [[TOK, nj], [0, TAIL], [1, T]])).then_inc(xb_in[g], 16)

            def load_w(l, w, bias):
                wt, k = w.tensor, HID * O
                st = stage(L12_SPLIT)
                c0 = WHOLE_CHUNKS
                sp.dma_start(w_whole[l][0:MAIN, :, :], bass.AP(wt, 0, [[O, MAIN], [k, c0], [1, O]])).then_inc(w_whole_in, 16)
                sp.dma_start(w_whole[l][MAIN:P, :, :],
                             bass.AP(wt, CHUNKS * k, [[O, P - MAIN], [k, c0], [1, O]])).then_inc(w_whole_in, 16)
                sp.dma_start(st[0:MAIN, :, :], bass.AP(wt, c0 * k, [[O, MAIN], [k, L12_SPLIT], [1, O]])).then_inc(w_in[l], 16)
                for g in range(GROUPS - 1):
                    a = c0 if g == 0 else GROUP * g
                    n = GROUP * (g + 1) - a
                    sp.dma_start(st[MAIN:P, a - c0:a - c0 + n, :],
                                 bass.AP(wt, (CHUNKS + a % GROUP) * k + 32 * g * O, [[O, P - MAIN], [k, n], [1, O]]))\
                      .then_inc(w_in[l], 16)
                b_at = BIAS_CHUNK - c0
                for j in range(TAIL_M):
                    n = len(range(j, F, TAIL_M))
                    at = MAIN + TAIL * j
                    sp.dma_start(st[at:at + TAIL, b_at:b_at + n, :],
                                 bass.AP(wt, j * k + MAIN * O, [[O, TAIL], [TAIL_M * k, n], [1, O]])).then_inc(w_in[l], 16)
                sp.dma_start(st[ONES_ROW:ONES_ROW + 1, b_at, :], bass.AP(bias.tensor, 0, [[O, 1], [1, O]])).then_inc(w_in[l], 16)

            turn_x(0)
            n2 = XROWS - F
            sp.dma_start(bass.AP(w0c_t, 0, [[2 * F * O, F], [1, F * O]]), bass.AP(w0, 0, [[F * O, F], [1, F * O]])).then_inc(w0_again[0], 16)
            sp.dma_start(bass.AP(w0c_t, F * O, [[2 * F * O, F], [1, n2 * O]]), bass.AP(w0, 0, [[F * O, F], [1, n2 * O]])).then_inc(w0_again[0], 16)
            sp.dma_start(bass.AP(w0r_t, 0, [[F * O, F], [1, F * O]]), bass.AP(w0, 0, [[F * O, F], [1, F * O]])).then_inc(w0_again[1], 16)
            sp.dma_start(bass.AP(w0r_t, F * F * O, [[F * O, n2], [1, F * O]]), bass.AP(w0, 0, [[F * O, n2], [1, F * O]])).then_inc(w0_again[1], 16)
            sp.wait_ge(xt_done, 32)
            sp.wait_ge(ones_l0, 2)
            load_pairs(0)
            turn_x(1)
            sp.wait_ge(cleared, 3)
            sp.wait_ge(w0_again[0], 32)
            sp.wait_ge(w0_again[1], 32)
            for k in range(SHIFTS):
                last = len(range(k, L0_PAIRS, SHIFTS))
                at = slice(k * F, (k + 1) * F)
                sp.dma_start(pair_w[at, 0:last, :],
                             bass.AP(w0c_t, k * O, [[(2 * F + 1) * O, F], [SHIFTS * O, last], [1, O]])).then_inc(w_in[0], 16)
                c = 1 if k == 0 else 0
                sp.dma_start(pair_w2[at, c:last, :],
                             bass.AP(w0r_t, (k + SHIFTS * c) * F * O, [[(F + 1) * O, F], [SHIFTS * F * O, last - c], [1, O]]))\
                  .then_inc(w_in[0], 16)
            sp.dma_start(pair_w[L0_ONES:L0_ROWS, 0, :], bass.AP(b0.tensor, 0, [[O, 1], [1, O]])).then_inc(w_in[0], 16)
            load_w(1, W1, b1)
            sp.wait_ge(w_low_done, 2)
            sp.wait_ge(wz, 1)
            load_w(2, W2, b2)
            sp.wait_ge(xt_done, 64)
            turn_x(2)
            sp.wait_ge(product, SPLITS[0])
            load_pairs(1)
            sp.wait_ge(ones_set, 1)
            for g in range(GROUPS):
                load_xb(0, g)

            def tail(layer, blk):
                h = hid[layer]
                sp.wait_ge(hid_in[layer], 3 * blk + 2)
                for j in range(1, TAIL_M):
                    sp.dma_start(h[MAIN + TAIL * j:MAIN + TAIL * (j + 1), GROUPS - 1, :], h[MAIN:MAIN + TAIL, GROUPS - 1, :])\
                        .then_inc(tail_in[layer], 16)

            def send(l, blk):
                sp.wait_ge(o_in[l], blk + 1)
                c0 = OUT_AT[0] if l == 0 else OUT_AT[1]
                c1 = OUT_AT[1] if l == 0 else OUT_COLS
                sp.dma_start(bass.AP(out.tensor, blk * (BT * OUT_COLS) + c0, [[OUT_COLS, BT], [1, c1 - c0]]), o_row[l][:, :])\
                    .then_inc(o_out[l], 16)

            def loads(n, pairs, turn):
                sp.wait_ge(xt_done, 32 * (n + 3) if turn else 32 * BLOCKS)
                if turn:
                    turn_x(n + 3)
                if pairs:
                    sp.wait_ge(product, split_number(0, n + 1, SPLITS[0] - 1) + 1)
                    load_pairs(n + 2)
                tail(2, n)
                for g in range(GROUPS):
                    sp.wait_ge(product, split_number(2, n, 2 * g) + 1)
                    load_xb(n + 1, g)
                    if g == 1:
                        tail(1, n + 1)
                    if g == 2:
                        send(0, n + 1)
                send(2, n)

            tail(1, 0)
            send(0, 0)
            with sp.Fori(0, BLOCKS - 3) as n:
                loads(n, True, True)
            loads(BLOCKS - 3, True, False)
            loads(BLOCKS - 2, False, False)
            tail(2, BLOCKS - 1)
            send(2, BLOCKS - 1)
            sp.wait_ge(o_out[0], 16 * (BLOCKS + 1))
            sp.wait_ge(o_out[2], 16 * (BLOCKS + 1))

        @block.gpsimd
        def _(pool):
            pool.sem_inc(slots_freed, RING)
            pool.sem_inc(o_out[0], 16)
            pool.sem_inc(o_out[2], 16)
            nc.gpsimd.memset(ident[:, :], 0.0).then_inc(consts_step, 1)
            nc.gpsimd.memset(group_b[:, :, :], 1.0).then_inc(consts_step, 1)
            pool.wait_ge(consts_step, 2)
            nc.gpsimd.affine_select(out=ident[:, :], in_=ident[:, :], compare_op=ALU.not_equal, fill=1.0,
                                    base=0, pattern=[[-1, P]], channel_multiplier=1).then_inc(consts, 1)
            nc.gpsimd.affine_select(out=group_b[:, :, :], in_=group_b[:, :, :], compare_op=ALU.is_ge, fill=0.0,
                                    base=0, pattern=[[P, TILES], [-D, BT]], channel_multiplier=1).then_inc(consts_step, 1)
            pool.wait_ge(consts_step, 3)
            nc.gpsimd.affine_select(out=group_b[:, :, :], in_=group_b[:, :, :], compare_op=ALU.is_ge, fill=0.0,
                                    base=D - 1, pattern=[[-P, TILES], [D, BT]], channel_multiplier=-1).then_inc(consts, 1)

        @block.vector
        def _(dve):
            def zeros():
                tail_chunks = stage(L12_SPLIT)[MAIN:P, BIAS_CHUNK - WHOLE_CHUNKS:L12_SPLIT, :]
                return nc.vector.memset(tail_chunks, 0.0)

            nc.vector.memset(x_left[MAIN:P, :], 1.0).then_inc(ones_l0, 1)
            nc.vector.memset(x_right[MAIN:P, :, :], 1.0).then_inc(ones_l0, 1)
            for l in (1, 2):
                nc.vector.memset(hid[l][MAIN:P, GROUPS - 1, :], 1.0).then_inc(ones_hid, 1)
            nc.vector.memset(pair_w, 0.0).then_inc(cleared, 1)
            nc.vector.memset(pair_w2, 0.0).then_inc(cleared, 1)
            zeros().then_inc(cleared, 1)

            def low_w(l, st, rows=P):
                dve.wait_ge(w_high_done, l + 1)
                hi = w_split[l][0:rows, :, 0:O].bitcast(F32)
                nc.vector.tensor_tensor(w_split[l][0:rows, :, O:2 * O], st, hi, ALU.subtract).then_inc(w_low_done, 1)

            dve.wait_ge(w_in[0], 16 * 7)
            nc.vector.tensor_tensor(pair_w[0:L0_ROWS, :, :], pair_w[0:L0_ROWS, :, :], pair_w2[0:L0_ROWS, :, :], ALU.add)\
              .then_inc(pair_sum, 1)
            low_w(0, pair_w[0:L0_ROWS, :, :], L0_ROWS)

            def products(layer, blk, b):
                c0, n, is_whole = BATCHES[layer][b]
                if layer == 0:
                    if b == 0:
                        dve.wait_ge(pairs_in, 96 * (blk + 1))
                    left = x_left[0:L0_ROWS, :].unsqueeze(1).to_broadcast([L0_ROWS, n, T])
                    right = x_right[0:L0_ROWS, c0:c0 + n, :]
                    rows = L0_ROWS
                else:
                    g = c0 // GROUP
                    if c0 == 0:
                        dve.wait_ge(hid_in[layer], 3 * blk + 1)
                    if c0 == GROUP:
                        dve.wait_ge(hid_in[layer], 3 * blk + 3)
                    if c0 == GROUP * (GROUPS - 1):
                        dve.wait_ge(tail_in[layer], 16 * (TAIL_M - 1) * (blk + 1))
                    if layer == 1 and c0 % GROUP == 0:
                        dve.wait_ge(xb_in[g], XB_COUNT[g] * (blk + 1))
                    left = hid[layer][:, g, :].unsqueeze(1).to_broadcast([P, n, T])
                    right = xb[:, c0:c0 + n, :]
                    rows = P
                if is_whole:
                    dve.wait_ge(whole_used, whole_number(layer, blk))
                    dst = z_whole[0:rows, 0:n * T].rearrange("p (c t) -> p c t", t=T)
                    nc.vector.tensor_tensor(dst, left, right, ALU.mult).then_inc(whole, 1)
                else:
                    k = b - (layer > 0)
                    slot = ring_slot(layer, blk, k)
                    dve.wait_ge(slots_freed, split_number(layer, blk, k) + 1)
                    dst = z[0:rows, slot, 0:n * T].rearrange("p (c t) -> p c t", t=T)
                    nc.vector.tensor_tensor(dst, left, right, ALU.mult).then_inc(product, 1)

            def lows(layer, blk, b):
                c0, n, _ = BATCHES[layer][b]
                k = b - (layer > 0)
                rows = L0_ROWS if layer == 0 else P
                dve.wait_ge(high, split_number(layer, blk, k) + 1)
                slot = ring_slot(layer, blk, k)
                zz = z[0:rows, slot, 0:n * T]
                nc.vector.tensor_tensor(z_low[slot][0:rows, 0:n * T], zz, z_high[slot][0:rows, 0:n * T].bitcast(F32),
                                        ALU.subtract).then_inc(low, 1)

            def sums(layer, blk):
                for t in range(TILES):
                    dve.wait_ge(second_half[layer], TILES * blk + t + 1)
                    mine = s[layer][:, t, :]
                    nc.vector.tensor_tensor(mine, acc[layer][t][:, 0:O], mine, ALU.add).then_inc(s_in[layer], 1)

            dve.wait_ge(w_low_done, 1)
            products(0, 0, 0)
            products(0, 0, 1)
            lows(0, 0, 0)
            lows(0, 0, 1)
            low_w(1, stage(L12_SPLIT))
            dve.wait_ge(w_low_done, 2)
            zeros().then_inc(wz, 1)
            low_w(2, stage(L12_SPLIT))
            dve.wait_ge(w_low_done, 3)
            nc.vector.memset(xb[MAIN:P, BIAS_CHUNK:CHUNKS, :], 1.0).then_inc(ones_set, 1)
            sums(0, 0)
            pending = None
            for b in range(AHEAD):
                products(1, 0, b)
                if pending:
                    lows(*pending)
                pending = None if b == 0 else (1, 0, b)

            def step(n, more):
                pending = (1, n, AHEAD - 1)
                for layer, blk, b in order(n, more):
                    if (layer, b) == (2, 0):
                        if not more:
                            lows(*pending)
                            pending = None
                        sums(1, n)
                        if more:
                            lows(*pending)
                            pending = None
                    products(layer, blk, b)
                    if pending:
                        lows(*pending)
                        pending = None
                    if not BATCHES[layer][b][2]:
                        pending = (layer, blk, b)
                    if (layer, b) == (2, 2) and more:
                        sums(0, n + 1)
                    if (layer, b) == (1, 4):
                        sums(2, n)
                if not more:
                    lows(*pending)
                    sums(2, n)

            with dve.Fori(0, BLOCKS - 1) as n:
                step(n, True)
            step(BLOCKS - 1, False)

        @block.scalar
        def _(act):
            def high_w(l, st, rows=P):
                nc.scalar.activation(w_split[l][0:rows, :, 0:O], st, ACT.Copy).then_inc(w_high_done, 1)

            act.wait_ge(pair_sum, 1)
            high_w(0, pair_w[0:L0_ROWS, :, :], L0_ROWS)

            def highs(layer, blk, b):
                c0, n, _ = BATCHES[layer][b]
                k = b - (layer > 0)
                rows = L0_ROWS if layer == 0 else P
                number = split_number(layer, blk, k)
                slot = ring_slot(layer, blk, k)
                act.wait_ge(slots_freed, number + 1)
                act.wait_ge(product, number + 1)
                nc.scalar.activation(z_high[slot][0:rows, 0:n * T], z[0:rows, slot, 0:n * T],
                                     ACT.Copy).then_inc(high, 1)

            def hidden(layer, blk):
                h = hid[layer + 1]
                act.wait_ge(turned_in, transpose_number(layer, blk) + 1)
                nc.scalar.activation(h[0:MAIN, 0, :], turned[0:MAIN, 0:T], ACT.Relu)
                nc.scalar.activation(h[MAIN:P, 0, :], turned[0:P - MAIN, 0:T], ACT.Relu).then_inc(hid_in[layer + 1], 1)
                nc.scalar.activation(h[MAIN:HID, GROUPS - 1, :], turned[MAIN:HID, 0:T], ACT.Relu).then_inc(hid_in[layer + 1], 1)
                for g in range(1, GROUPS - 1):
                    nc.scalar.activation(h[MAIN:P, g, :], turned[32 * g:32 * (g + 1), 0:T], ACT.Relu)
                nc.scalar.activation(h[0:MAIN, 1:GROUPS, :], turned[0:MAIN, 0:T].unsqueeze(1).to_broadcast([MAIN, GROUPS - 1, T]),
                                     ACT.Relu).then_inc(hid_in[layer + 1], 1)

            def second_halves(layer, blk):
                for t in range(TILES):
                    if t == 0:
                        act.wait_ge(tile0[layer], blk + 1)
                    else:
                        act.wait_ge(slots_freed, RING + split_number(layer, blk, SPLITS[layer] - 1) + 1)
                    nc.scalar.activation(s[layer][:, t, :], acc[layer][t][:, O:2 * O], ACT.Copy).then_inc(second_half[layer], 1)

            def relu(layer, blk):
                act.wait_ge(s_in[layer], TILES * (blk + 1))
                a, b = DIRECT[layer]
                nc.scalar.activation(s[layer][:, :, a:b], s[layer][:, :, a:b], ACT.Relu).then_inc(relu_done[layer], 1)

            def results(l, blk):
                act.wait_ge(direct_summed[l], blk + 1)
                act.wait_ge(o_out[l], 16 * (blk + 1))
                c0 = OUT_AT[0] if l == 0 else OUT_AT[1]
                c1 = OUT_AT[1] if l == 0 else OUT_COLS
                nc.scalar.activation(o_row[l][:, :], summed[0:BT, c0:c1], ACT.Copy).then_inc(o_in[l], 1)

            highs(0, 0, 0)
            highs(0, 0, 1)
            act.wait_ge(w_in[1], 16 * 12)
            high_w(1, stage(L12_SPLIT))
            act.wait_ge(w_in[2], 16 * 12)
            high_w(2, stage(L12_SPLIT))
            second_halves(0, 0)
            act.wait_ge(ones_hid, 2)
            hidden(0, 0)
            relu(0, 0)
            results(0, 0)
            for b in range(1, AHEAD):
                highs(1, 0, b)

            def step(n, more):
                for layer, blk, b in order(n, more):
                    if (layer, b) == (2, 0):
                        second_halves(1, n)
                        hidden(1, n)
                        relu(1, n)
                    if not BATCHES[layer][b][2]:
                        highs(layer, blk, b)
                    if more:
                        if (layer, b) == (2, 1):
                            second_halves(0, n + 1)
                        if (layer, b) == (2, 2):
                            relu(0, n + 1)
                        if (layer, b) == (2, 4):
                            hidden(0, n + 1)
                        if (layer, b) == (2, 5):
                            results(0, n + 1)
                        if (layer, b) == (1, 3):
                            second_halves(2, n)
                        if (layer, b) == (1, 4):
                            relu(2, n)
                        if (layer, b) == (1, 5):
                            results(2, n)
                if not more:
                    second_halves(2, n)
                    relu(2, n)
                    results(2, n)

            with act.Fori(0, BLOCKS - 1) as n:
                step(n, True)
            step(BLOCKS - 1, False)

        @block.tensor
        def _(pe):
            def multiply(layer, blk, b, between=None):
                c0, n, is_whole = BATCHES[layer][b]
                chunks = L0_CHUNKS if layer == 0 else CHUNKS
                rows = L0_ROWS if layer == 0 else P
                k = b - (layer > 0)
                if is_whole:
                    pe.wait_ge(whole, whole_number(layer, blk) + 1)
                else:
                    pe.wait_ge(low, split_number(layer, blk, k) + 1)
                slot = None if is_whole else ring_slot(layer, blk, k)
                for c in range(c0, c0 + n):
                    if between and c == c0 + between[0]:
                        between[1]()
                    first, end = c == 0, c == chunks - 1
                    at = (c - c0) * T
                    for t in range(TILES):
                        a = acc[layer][t]
                        tok = slice(at + t * P, at + (t + 1) * P)
                        if is_whole:
                            last = nc.tensor.matmul(a[:, 0:O], z_whole[:, tok], w_whole[layer][:, c, :], start=first, stop=False,
                                                    skip_group_check=True)
                        else:
                            w = w_split[layer][0:rows, c - (WHOLE_CHUNKS if layer else 0), :]
                            nc.tensor.matmul(a[:, 0:2 * O], z_high[slot][0:rows, tok], w, start=first, stop=False,
                                             skip_group_check=True)
                            last = nc.tensor.matmul(a[:, 0:O], z_low[slot][0:rows, tok], w[:, 0:O], start=False, stop=end,
                                                    skip_group_check=True)
                            if end and t == 0:
                                last.then_inc(tile0[layer], 1)
                last.then_inc(whole_used if is_whole else slots_freed, 1)

            def transpose(layer, blk):
                pe.wait_ge(s_in[layer], TILES * (blk + 1))
                tn = transpose_number(layer, blk)
                if layer == 1:
                    pe.wait_ge(hid_in[1], 3 * blk + 3)
                else:
                    pe.wait_ge(hid_in[2], 3 * blk)
                for t in range(TILES):
                    last = nc.tensor.transpose(turned[0:HID, t * P:(t + 1) * P], s[layer][:, t, 0:HID], ident[:, :])
                last.then_inc(turned_in, 1)

            def sum_over_d(layer, blk):
                pe.wait_ge(relu_done[layer], blk + 1)
                a, b = DIRECT[layer]
                at = OUT_AT[layer]
                for t in range(TILES):
                    last = nc.tensor.matmul(summed[0:BT, at:at + b - a], group_b[:, t, :], s[layer][:, t, a:b],
                                            start=(t == 0), stop=(t == TILES - 1), skip_group_check=True)
                last.then_inc(direct_summed[layer], 1)

            pe.wait_ge(w_low_done, 1)
            pe.wait_ge(consts, 2)
            multiply(0, 0, 0)
            multiply(0, 0, 1)
            transpose(0, 0)
            sum_over_d(0, 0)
            pe.wait_ge(w_low_done, 3)
            pe.wait_ge(w_whole_in, 64)

            for b in range(AHEAD):
                multiply(1, 0, b)

            def step(n, more):
                for layer, blk, b in order(n, more):
                    if not more and (layer, b) == (2, 0):
                        transpose(1, n)
                    multiply(layer, blk, b, (3, lambda: transpose(1, n)) if (layer, b) == (0, 0) else None)
                    if (layer, b) == (2, 0):
                        sum_over_d(1, n)
                    if more:
                        if (layer, b) == (2, 2):
                            transpose(0, n + 1)
                            sum_over_d(0, n + 1)
                        if (layer, b) == (1, 2):
                            sum_over_d(2, n)
                if not more:
                    sum_over_d(2, n)

            with pe.Fori(0, BLOCKS - 1) as n:
                step(n, True)
            step(BLOCKS - 1, False)


_INS = ["r_x", "L0_rec_W0", "L0_rec_W1", "L0_rec_W2", "L0_rec_b0", "L0_rec_b1", "L0_rec_b2"]
_OUTS = [((B, OUT_COLS), "float32")]


def kernel(**inputs):
    import numpy as _np
    import concourse.bacc as _bacc
    from concourse import mybir as _mybir
    from concourse.bass_utils import run_bass_kernel_spmd as _run

    nc = _bacc.Bacc("TRN2", target_bir_lowering=False, num_devices=1)
    arrays, args = {}, []
    for name in _INS:
        a = _np.ascontiguousarray(inputs[name])
        arrays[f"in_{name}_dram"] = a
        args.append(nc.dram_tensor(f"in_{name}_dram", a.shape, _mybir.dt.from_np(a.dtype), kind="ExternalInput").ap())
    for i, (shape, dtype) in enumerate(_OUTS):
        dt = _mybir.dt.from_np(_np.dtype(dtype))
        args.append(nc.dram_tensor(f"out_{i}_dram", shape, dt, kind="ExternalOutput").ap())
    cin_kernel(nc, *args)
    r = _run(nc, [arrays], core_ids=[0])
    return r.results[0]["out_0_dram"]
```

```python
from contextlib import ExitStack

import concourse.bass as bass
from concourse import mybir

F32 = mybir.dt.float32
F32R = mybir.dt.float32r
ALU = mybir.AluOpType
ACT = mybir.ActivationFunctionType

P = 128
B, F, D = 512, 39, 32
O = 200
HID = 100
T = 256
TILES = T // P
BT = T // D
BLOCKS = B * D // T
TOK = B * D

SHIFTS = 3
L0_ONES = SHIFTS * F
L0_ROWS = L0_ONES + 1
L0_PAIRS = (F + 1) // 2
L0_CHUNKS = -(-L0_PAIRS // SHIFTS)
XROWS = F + SHIFTS * L0_CHUNKS - 1

MAIN = 96
TAIL = HID - MAIN
CHUNKS = 31
GROUP = 8
GROUPS = 4
TAIL_M = 7
TAIL_CHUNKS = -(-F // TAIL_M)
ONES_ROW = MAIN + TAIL_M * TAIL
BIAS_CHUNK = GROUP * (GROUPS - 1)

BATCH = 4
L0_BATCHES = [(0, 4), (4, 3)]
WHOLE = {0: 0, 1: 1, 2: 1}
L12_BATCHES = [(c, min(BATCH, CHUNKS - c)) for c in range(0, CHUNKS, BATCH)]
BATCHES = {0: L0_BATCHES, 1: L12_BATCHES, 2: L12_BATCHES}
SPLITS = {l: len(BATCHES[l]) - WHOLE[l] for l in BATCHES}
WHOLE_CHUNKS = {l: BATCH * WHOLE[l] for l in WHOLE}
SPLIT_CHUNKS = {0: L0_CHUNKS, 1: CHUNKS - WHOLE_CHUNKS[1], 2: CHUNKS - WHOLE_CHUNKS[2]}
STAGED = max(SPLIT_CHUNKS[1], SPLIT_CHUNKS[2])
WHOLE_PER_BLOCK = WHOLE[1] + WHOLE[2]
WHOLE_RING = 1
RING = 4
PER_BLOCK = SPLITS[0] + SPLITS[1] + SPLITS[2]
AHEAD = 6
DIRECT = {0: (HID, O), 1: (HID, O), 2: (0, O)}
OUT_AT = {0: 0, 1: HID, 2: 2 * HID}
OUT_COLS = 4 * HID


def split_number(layer, blk, k):
    if layer == 0:
        return k if isinstance(blk, int) and blk == 0 else SPLITS[0] + PER_BLOCK * (blk - 1) + SPLITS[1] + k
    if layer == 1:
        return SPLITS[0] + PER_BLOCK * blk + k
    last = isinstance(blk, int) and blk == BLOCKS - 1
    return SPLITS[0] + PER_BLOCK * blk + SPLITS[1] + (0 if last else SPLITS[0]) + k


def ring_slot(layer, blk, k):
    assert PER_BLOCK % RING == 0
    if layer == 0:
        first = 0 if isinstance(blk, int) and blk == 0 else SPLITS[0] + SPLITS[1]
        return (first + k) % RING
    if layer == 1:
        return (SPLITS[0] + k) % RING
    return split_number(2, blk if isinstance(blk, int) else 0, k) % RING


def whole_number(layer, blk, b):
    return WHOLE_PER_BLOCK * blk + (layer - 1) * WHOLE[1] + b


def transpose_number(layer, blk):
    return 2 * blk + layer


def order(n, more):
    turn = [(1, n, b) for b in range(AHEAD, len(L12_BATCHES))]
    if more:
        turn += [(0, n + 1, b) for b in range(len(L0_BATCHES))]
    turn += [(2, n, b) for b in range(len(L12_BATCHES))]
    if more:
        turn += [(1, n + 1, b) for b in range(AHEAD)]
    return turn


def cin_kernel(nc, r_x, W0, W1, W2, b0, b1, b2, out):
    x, w0 = r_x.tensor, W0.tensor
    xt = nc.dram_tensor("x_by_field", [XROWS, TOK], F32)
    w0c = nc.dram_tensor("w0_columns_again", [F, 2 * F, O], F32)
    w0r = nc.dram_tensor("w0_rows_again", [2 * F, F, O], F32)
    xt_t, w0c_t, w0r_t = xt.ap().tensor, w0c.ap().tensor, w0r.ap().tensor

    with ExitStack() as ctx:
        def sb(name, shape, dt=F32):
            return ctx.enter_context(nc.sbuf_tensor(name, shape, dt))

        def bank(name):
            return ctx.enter_context(nc.psum_tensor(name, [P, 512], F32))

        def sem(name):
            return ctx.enter_context(nc.semaphore(name))

        w_split = {l: sb(f"w_split{l}", [P, n, 2 * O], F32R) for l, n in SPLIT_CHUNKS.items()}
        w_whole = {l: sb(f"w_whole{l}", [P, n, O]) for l, n in WHOLE_CHUNKS.items() if n}
        xb = sb("xb", [P, CHUNKS, T])
        staged = xb[:, :, :].rearrange("p c t -> p (c t)")
        x_left = sb("x_left", [P, T])
        x_right = sb("x_right", [P, L0_CHUNKS, T])
        hid = {1: sb("hid1", [P, GROUPS, T]), 2: sb("hid2", [P, GROUPS, T])}
        z = sb("z", [P, RING, BATCH * T])
        z_whole = [sb(f"z_whole{i}", [P, BATCH * T]) for i in range(WHOLE_RING)]
        z_high = [sb(f"z_high{i}", [P, BATCH * T], F32R) for i in range(RING)]
        z_low = [sb(f"z_low{i}", [P, BATCH * T], F32R) for i in range(RING)]
        s = {l: sb(f"s{l}", [P, TILES, O]) for l in range(3)}
        ident = sb("ident", [P, P])
        group_b = sb("group_b", [P, TILES, BT])
        o_row = {0: sb("o_row0", [BT, HID]), 2: sb("o_row12", [BT, OUT_COLS - HID])}

        acc = {l: [bank(f"acc{l}{t}") for t in range(TILES)] for l in range(3)}
        turned = bank("turned")
        summed = bank("summed")

        xt_done = sem("xt_done")
        w0_again = [sem("w0c_done"), sem("w0r_done")]
        pairs_in = sem("pairs_in")
        xb_in = [sem(f"xb_in{g}") for g in range(GROUPS)]
        XB_COUNT = [32] * (GROUPS - 1) + [16 + 16 * TAIL_CHUNKS]
        pairs_w_in = sem("pairs_w_in")
        w_in = {l: [sem(f"w_in{l}_{g}") for g in range(GROUPS)] for l in (1, 2)}
        W_COUNT = [32] * (GROUPS - 1) + [16 * (2 + TAIL_M)]
        w_whole_in = sem("w_whole_in")
        cleared = sem("cleared")
        wz = sem("wz")
        pair_sum = sem("pair_sum")
        w_high_done = sem("w_high_done")
        w_low_done = sem("w_low_done")
        ones_set = sem("ones_set")
        ones_l0 = sem("ones_l0")
        ones_hid = sem("ones_hid")
        consts = sem("consts")
        consts_step = sem("consts_step")
        product = sem("product")
        whole = sem("whole")
        high = sem("high")
        low = sem("low")
        slots_freed = sem("slots_freed")
        whole_used = sem("whole_used")
        tile0 = [sem(f"tile0_{l}") for l in range(3)]
        second_half = [sem(f"second_half{l}") for l in range(3)]
        s_in = [sem(f"s_in{l}") for l in range(3)]
        relu_done = [sem(f"relu{l}") for l in range(3)]
        turned_in = sem("turned_in")
        hid_in = {1: sem("hid1_in"), 2: sem("hid2_in")}
        tail_in = {1: sem("tail1_in"), 2: sem("tail2_in")}
        direct_summed = [sem(f"direct_summed{l}") for l in range(3)]
        o_in = {0: sem("o0_in"), 2: sem("o12_in")}
        o_out = {0: sem("o0_out"), 2: sem("o12_out")}

        block = ctx.enter_context(nc.Block())

        Q_AT = STAGED * O

        assert SPLIT_CHUNKS[2] * O <= BIAS_CHUNK * T

        def stage(l):
            return staged[:, 0:SPLIT_CHUNKS[l] * O].rearrange("p (c o) -> p c o", o=O)

        def piece(l, g):
            a = max(GROUP * g, WHOLE_CHUNKS[l])
            return a, min(GROUP * (g + 1), CHUNKS) - a

        def pieces(l):
            return [g for g in range(GROUPS) if piece(l, g)[1] > 0]

        def piece_number(l, g):
            return 1 + (len(pieces(1)) if l == 2 else 0) + pieces(l).index(g)

        pair_w = z[:, :, :].rearrange("p a b -> p (a b)")[:, 0:L0_CHUNKS * O].rearrange("p (c o) -> p c o", o=O)
        pair_w2 = staged[:, Q_AT:Q_AT + L0_CHUNKS * O].rearrange("p (c o) -> p c o", o=O)

        @block.sync
        def _(sp):
            def turn_x(blk):
                src = [[D, F], [F * D, BT], [1, D]]
                dst = [[TOK, F], [D, BT], [1, D]]
                n2 = XROWS - F
                sp.dma_start(bass.AP(xt_t, blk * T, dst), bass.AP(x, blk * (BT * F * D), src)).then_inc(xt_done, 16)
                sp.dma_start(bass.AP(xt_t, blk * T + F * TOK, [[TOK, n2]] + dst[1:]),
                             bass.AP(x, blk * (BT * F * D), [[D, n2]] + src[1:])).then_inc(xt_done, 16)

            def load_pairs(blk):
                for k in range(SHIFTS):
                    at = slice(k * F, (k + 1) * F)
                    sp.dma_start(x_left[at, :], bass.AP(xt_t, blk * T, [[TOK, F], [1, T]])).then_inc(pairs_in, 16)
                    sp.dma_start(x_right[at, :, :],
                                 bass.AP(xt_t, blk * T + k * TOK, [[TOK, F], [SHIFTS * TOK, L0_CHUNKS], [1, T]]))\
                      .then_inc(pairs_in, 16)

            def load_xb(blk, g):
                n = min(GROUP, CHUNKS - GROUP * g)
                sp.dma_start(xb[0:MAIN, GROUP * g:GROUP * g + n, :],
                             bass.AP(xt_t, blk * T + GROUP * g * TOK, [[0, MAIN], [TOK, n], [1, T]])).then_inc(xb_in[g], 16)
                if g < GROUPS - 1:
                    sp.dma_start(xb[MAIN:P, GROUP * g:GROUP * g + n, :],
                                 bass.AP(xt_t, blk * T + CHUNKS * TOK, [[0, P - MAIN], [TOK, n], [1, T]])).then_inc(xb_in[g], 16)
                else:
                    for i in range(TAIL_CHUNKS):
                        nj = min(TAIL_M, F - TAIL_M * i)
                        sp.dma_start(xb[MAIN:MAIN + TAIL * nj, BIAS_CHUNK + i, :],
                                     bass.AP(xt_t, blk * T + TAIL_M * i * TOK, [[TOK, nj], [0, TAIL], [1, T]])).then_inc(xb_in[g], 16)

            def load_w_whole(l, w):
                k, n = HID * O, WHOLE_CHUNKS[l]
                sp.dma_start(w_whole[l][0:MAIN, :, :], bass.AP(w.tensor, 0, [[O, MAIN], [k, n], [1, O]])).then_inc(w_whole_in, 16)
                sp.dma_start(w_whole[l][MAIN:P, :, :],
                             bass.AP(w.tensor, CHUNKS * k, [[O, P - MAIN], [k, n], [1, O]])).then_inc(w_whole_in, 16)

            def load_w(l, w, bias, g):
                a, n = piece(l, g)
                wt, k = w.tensor, HID * O
                st = stage(l)
                at = a - WHOLE_CHUNKS[l]
                sp.dma_start(st[0:MAIN, at:at + n, :], bass.AP(wt, a * k, [[O, MAIN], [k, n], [1, O]])).then_inc(w_in[l][g], 16)
                if g < GROUPS - 1:
                    sp.dma_start(st[MAIN:P, at:at + n, :],
                                 bass.AP(wt, (CHUNKS + a % GROUP) * k + 32 * g * O, [[O, P - MAIN], [k, n], [1, O]]))\
                      .then_inc(w_in[l][g], 16)
                else:
                    for j in range(TAIL_M):
                        n = len(range(j, F, TAIL_M))
                        row = MAIN + TAIL * j
                        sp.dma_start(st[row:row + TAIL, at:at + n, :],
                                     bass.AP(wt, j * k + MAIN * O, [[O, TAIL], [TAIL_M * k, n], [1, O]])).then_inc(w_in[l][g], 16)
                    sp.dma_start(st[ONES_ROW:ONES_ROW + 1, at, :], bass.AP(bias.tensor, 0, [[O, 1], [1, O]])).then_inc(w_in[l][g], 16)

            turn_x(0)
            n2 = XROWS - F
            sp.dma_start(bass.AP(w0c_t, 0, [[2 * F * O, F], [1, F * O]]), bass.AP(w0, 0, [[F * O, F], [1, F * O]])).then_inc(w0_again[0], 16)
            sp.dma_start(bass.AP(w0c_t, F * O, [[2 * F * O, F], [1, n2 * O]]), bass.AP(w0, 0, [[F * O, F], [1, n2 * O]])).then_inc(w0_again[0], 16)
            sp.dma_start(bass.AP(w0r_t, 0, [[F * O, F], [1, F * O]]), bass.AP(w0, 0, [[F * O, F], [1, F * O]])).then_inc(w0_again[1], 16)
            sp.dma_start(bass.AP(w0r_t, F * F * O, [[F * O, n2], [1, F * O]]), bass.AP(w0, 0, [[F * O, n2], [1, F * O]])).then_inc(w0_again[1], 16)
            sp.wait_ge(xt_done, 32)
            sp.wait_ge(ones_l0, 2)
            load_pairs(0)
            turn_x(1)
            sp.wait_ge(cleared, 3)
            sp.wait_ge(w0_again[0], 32)
            sp.wait_ge(w0_again[1], 32)
            for k in range(SHIFTS):
                last = len(range(k, L0_PAIRS, SHIFTS))
                at = slice(k * F, (k + 1) * F)
                sp.dma_start(pair_w[at, 0:last, :],
                             bass.AP(w0c_t, k * O, [[(2 * F + 1) * O, F], [SHIFTS * O, last], [1, O]])).then_inc(pairs_w_in, 16)
                c = 1 if k == 0 else 0
                sp.dma_start(pair_w2[at, c:last, :],
                             bass.AP(w0r_t, (k + SHIFTS * c) * F * O, [[(F + 1) * O, F], [SHIFTS * F * O, last - c], [1, O]]))\
                  .then_inc(pairs_w_in, 16)
            sp.dma_start(pair_w[L0_ONES:L0_ROWS, 0, :], bass.AP(b0.tensor, 0, [[O, 1], [1, O]])).then_inc(pairs_w_in, 16)
            for g in pieces(1):
                load_w(1, W1, b1, g)
            for l, w in ((1, W1), (2, W2)):
                if WHOLE[l]:
                    load_w_whole(l, w)
            for g in pieces(2):
                a, n = piece(2, g)
                last = a + n - 1 - WHOLE_CHUNKS[2] + WHOLE_CHUNKS[1]
                sp.wait_ge(w_low_done, piece_number(1, last // GROUP) + 1)
                if g == GROUPS - 1:
                    sp.wait_ge(wz, 1)
                load_w(2, W2, b2, g)
            sp.wait_ge(xt_done, 64)
            turn_x(2)
            sp.wait_ge(product, SPLITS[0])
            load_pairs(1)
            for g in range(GROUPS):
                chunk = min(-(-GROUP * (g + 1) * T // O), SPLIT_CHUNKS[2]) - 1 + WHOLE_CHUNKS[2]
                sp.wait_ge(w_low_done, piece_number(2, chunk // GROUP) + 1)
                if g == GROUPS - 1:
                    sp.wait_ge(ones_set, 1)
                load_xb(0, g)

            def tail(layer, blk):
                h = hid[layer]
                sp.wait_ge(hid_in[layer], 3 * blk + 2)
                for j in range(1, TAIL_M):
                    sp.dma_start(h[MAIN + TAIL * j:MAIN + TAIL * (j + 1), GROUPS - 1, :], h[MAIN:MAIN + TAIL, GROUPS - 1, :])\
                        .then_inc(tail_in[layer], 16)

            def send(l, blk):
                sp.wait_ge(o_in[l], blk + 1)
                c0 = OUT_AT[0] if l == 0 else OUT_AT[1]
                c1 = OUT_AT[1] if l == 0 else OUT_COLS
                sp.dma_start(bass.AP(out.tensor, blk * (BT * OUT_COLS) + c0, [[OUT_COLS, BT], [1, c1 - c0]]), o_row[l][:, :])\
                    .then_inc(o_out[l], 16)

            def loads(n, pairs, turn):
                sp.wait_ge(xt_done, 32 * (n + 3) if turn else 32 * BLOCKS)
                if turn:
                    turn_x(n + 3)
                if pairs:
                    sp.wait_ge(product, split_number(0, n + 1, SPLITS[0] - 1) + 1)
                    load_pairs(n + 2)
                tail(2, n)
                for g in range(GROUPS):
                    b = 2 * g + 1
                    if b < WHOLE[2]:
                        sp.wait_ge(whole, whole_number(2, n, b) + 1)
                    else:
                        sp.wait_ge(product, split_number(2, n, b - WHOLE[2]) + 1)
                    load_xb(n + 1, g)
                    if g == 1:
                        tail(1, n + 1)
                    if g == 2:
                        send(0, n + 1)
                send(2, n)

            tail(1, 0)
            send(0, 0)
            with sp.Fori(0, BLOCKS - 3) as n:
                loads(n, True, True)
            loads(BLOCKS - 3, True, False)
            loads(BLOCKS - 2, False, False)
            tail(2, BLOCKS - 1)
            send(2, BLOCKS - 1)
            sp.wait_ge(o_out[0], 16 * (BLOCKS + 1))
            sp.wait_ge(o_out[2], 16 * (BLOCKS + 1))

        @block.gpsimd
        def _(pool):
            pool.sem_inc(slots_freed, RING)
            pool.sem_inc(whole_used, WHOLE_RING)
            pool.sem_inc(o_out[0], 16)
            pool.sem_inc(o_out[2], 16)
            nc.gpsimd.memset(ident[:, :], 0.0).then_inc(consts_step, 1)
            nc.gpsimd.memset(group_b[:, :, :], 1.0).then_inc(consts_step, 1)
            pool.wait_ge(consts_step, 2)
            nc.gpsimd.affine_select(out=ident[:, :], in_=ident[:, :], compare_op=ALU.not_equal, fill=1.0,
                                    base=0, pattern=[[-1, P]], channel_multiplier=1).then_inc(consts, 1)
            nc.gpsimd.affine_select(out=group_b[:, :, :], in_=group_b[:, :, :], compare_op=ALU.is_ge, fill=0.0,
                                    base=0, pattern=[[P, TILES], [-D, BT]], channel_multiplier=1).then_inc(consts_step, 1)
            pool.wait_ge(consts_step, 3)
            nc.gpsimd.affine_select(out=group_b[:, :, :], in_=group_b[:, :, :], compare_op=ALU.is_ge, fill=0.0,
                                    base=D - 1, pattern=[[-P, TILES], [D, BT]], channel_multiplier=-1).then_inc(consts, 1)

        @block.vector
        def _(dve):
            def zeros(l):
                at = BIAS_CHUNK - WHOLE_CHUNKS[l]
                return nc.vector.memset(stage(l)[MAIN:P, at:SPLIT_CHUNKS[l], :], 0.0)

            nc.vector.memset(x_left[MAIN:P, :], 1.0).then_inc(ones_l0, 1)
            nc.vector.memset(x_right[MAIN:P, :, :], 1.0).then_inc(ones_l0, 1)
            for l in (1, 2):
                nc.vector.memset(hid[l][MAIN:P, GROUPS - 1, :], 1.0).then_inc(ones_hid, 1)
            nc.vector.memset(pair_w, 0.0).then_inc(cleared, 1)
            nc.vector.memset(pair_w2, 0.0).then_inc(cleared, 1)
            zeros(1).then_inc(cleared, 1)

            def low_w(l, number, dst, st):
                dve.wait_ge(w_high_done, number + 1)
                nc.vector.tensor_tensor(dst[:, :, O:2 * O], st, dst[:, :, 0:O].bitcast(F32), ALU.subtract).then_inc(w_low_done, 1)

            dve.wait_ge(pairs_w_in, 16 * 7)
            nc.vector.tensor_tensor(pair_w[0:L0_ROWS, :, :], pair_w[0:L0_ROWS, :, :], pair_w2[0:L0_ROWS, :, :], ALU.add)\
              .then_inc(pair_sum, 1)
            low_w(0, 0, w_split[0][0:L0_ROWS, :, :], pair_w[0:L0_ROWS, :, :])

            def products(layer, blk, b):
                c0, n = BATCHES[layer][b]
                is_whole = b < WHOLE[layer]
                if layer == 0:
                    if b == 0:
                        dve.wait_ge(pairs_in, 96 * (blk + 1))
                    left = x_left[0:L0_ROWS, :].unsqueeze(1).to_broadcast([L0_ROWS, n, T])
                    right = x_right[0:L0_ROWS, c0:c0 + n, :]
                    rows = L0_ROWS
                else:
                    g = c0 // GROUP
                    if c0 == 0:
                        dve.wait_ge(hid_in[layer], 3 * blk + 1)
                    if c0 == GROUP:
                        dve.wait_ge(hid_in[layer], 3 * blk + 3)
                    if c0 == GROUP * (GROUPS - 1):
                        dve.wait_ge(tail_in[layer], 16 * (TAIL_M - 1) * (blk + 1))
                    if layer == 1 and c0 % GROUP == 0:
                        dve.wait_ge(xb_in[g], XB_COUNT[g] * (blk + 1))
                    left = hid[layer][:, g, :].unsqueeze(1).to_broadcast([P, n, T])
                    right = xb[:, c0:c0 + n, :]
                    rows = P
                if is_whole:
                    dve.wait_ge(whole_used, whole_number(layer, blk, b) + 1)
                    dst = z_whole[whole_number(layer, 0, b) % WHOLE_RING][0:rows, 0:n * T].rearrange("p (c t) -> p c t", t=T)
                    nc.vector.tensor_tensor(dst, left, right, ALU.mult).then_inc(whole, 1)
                else:
                    k = b - WHOLE[layer]
                    slot = ring_slot(layer, blk, k)
                    dve.wait_ge(slots_freed, split_number(layer, blk, k) + 1)
                    dst = z[0:rows, slot, 0:n * T].rearrange("p (c t) -> p c t", t=T)
                    nc.vector.tensor_tensor(dst, left, right, ALU.mult).then_inc(product, 1)

            def lows(layer, blk, b):
                c0, n = BATCHES[layer][b]
                k = b - WHOLE[layer]
                rows = L0_ROWS if layer == 0 else P
                dve.wait_ge(high, split_number(layer, blk, k) + 1)
                slot = ring_slot(layer, blk, k)
                zz = z[0:rows, slot, 0:n * T]
                nc.vector.tensor_tensor(z_low[slot][0:rows, 0:n * T], zz, z_high[slot][0:rows, 0:n * T].bitcast(F32),
                                        ALU.subtract).then_inc(low, 1)

            def sums(layer, blk):
                for t in range(TILES):
                    dve.wait_ge(second_half[layer], TILES * blk + t + 1)
                    mine = s[layer][:, t, :]
                    nc.vector.tensor_tensor(mine, acc[layer][t][:, 0:O], mine, ALU.add).then_inc(s_in[layer], 1)

            dve.wait_ge(w_low_done, 1)
            products(0, 0, 0)
            products(0, 0, 1)
            lows(0, 0, 0)
            lows(0, 0, 1)
            for l in (1, 2):
                for g in pieces(l):
                    a, n = piece(l, g)
                    at = slice(a - WHOLE_CHUNKS[l], a - WHOLE_CHUNKS[l] + n)
                    low_w(l, piece_number(l, g), w_split[l][:, at, :], stage(l)[:, at, :])
                if l == 1:
                    dve.wait_ge(w_low_done, piece_number(1, GROUPS - 1) + 1)
                    zeros(2).then_inc(wz, 1)
                    nc.vector.memset(xb[MAIN:P, BIAS_CHUNK:CHUNKS, :], 1.0).then_inc(ones_set, 1)
            sums(0, 0)
            pending = None
            for b in range(AHEAD):
                products(1, 0, b)
                if pending:
                    lows(*pending)
                pending = (1, 0, b) if b >= WHOLE[1] else None

            def step(n, more):
                pending = (1, n, AHEAD - 1)
                for layer, blk, b in order(n, more):
                    if (layer, b) == (2, 0):
                        if not more:
                            lows(*pending)
                            pending = None
                        sums(1, n)
                        if more:
                            lows(*pending)
                            pending = None
                    products(layer, blk, b)
                    if pending:
                        lows(*pending)
                        pending = None
                    if b >= WHOLE[layer]:
                        pending = (layer, blk, b)
                    if (layer, b) == (2, 2) and more:
                        sums(0, n + 1)
                    if (layer, b) == (1, 4):
                        sums(2, n)
                if not more:
                    lows(*pending)
                    sums(2, n)

            with dve.Fori(0, BLOCKS - 1) as n:
                step(n, True)
            step(BLOCKS - 1, False)

        @block.scalar
        def _(act):
            def high_w(dst, st):
                nc.scalar.activation(dst[:, :, 0:O], st, ACT.Copy).then_inc(w_high_done, 1)

            act.wait_ge(pair_sum, 1)
            high_w(w_split[0][0:L0_ROWS, :, :], pair_w[0:L0_ROWS, :, :])

            def highs(layer, blk, b):
                c0, n = BATCHES[layer][b]
                k = b - WHOLE[layer]
                rows = L0_ROWS if layer == 0 else P
                number = split_number(layer, blk, k)
                slot = ring_slot(layer, blk, k)
                act.wait_ge(slots_freed, number + 1)
                act.wait_ge(product, number + 1)
                nc.scalar.activation(z_high[slot][0:rows, 0:n * T], z[0:rows, slot, 0:n * T],
                                     ACT.Copy).then_inc(high, 1)

            def hidden(layer, blk):
                h = hid[layer + 1]
                act.wait_ge(turned_in, transpose_number(layer, blk) + 1)
                nc.scalar.activation(h[0:MAIN, 0, :], turned[0:MAIN, 0:T], ACT.Relu)
                nc.scalar.activation(h[MAIN:P, 0, :], turned[0:P - MAIN, 0:T], ACT.Relu).then_inc(hid_in[layer + 1], 1)
                nc.scalar.activation(h[MAIN:HID, GROUPS - 1, :], turned[MAIN:HID, 0:T], ACT.Relu).then_inc(hid_in[layer + 1], 1)
                for g in range(1, GROUPS - 1):
                    nc.scalar.activation(h[MAIN:P, g, :], turned[32 * g:32 * (g + 1), 0:T], ACT.Relu)
                nc.scalar.activation(h[0:MAIN, 1:GROUPS, :], turned[0:MAIN, 0:T].unsqueeze(1).to_broadcast([MAIN, GROUPS - 1, T]),
                                     ACT.Relu).then_inc(hid_in[layer + 1], 1)

            def second_halves(layer, blk):
                for t in range(TILES):
                    if t == 0:
                        act.wait_ge(tile0[layer], blk + 1)
                    else:
                        act.wait_ge(slots_freed, RING + split_number(layer, blk, SPLITS[layer] - 1) + 1)
                    nc.scalar.activation(s[layer][:, t, :], acc[layer][t][:, O:2 * O], ACT.Copy).then_inc(second_half[layer], 1)

            def relu(layer, blk):
                act.wait_ge(s_in[layer], TILES * (blk + 1))
                a, b = DIRECT[layer]
                nc.scalar.activation(s[layer][:, :, a:b], s[layer][:, :, a:b], ACT.Relu).then_inc(relu_done[layer], 1)

            def results(l, blk):
                act.wait_ge(direct_summed[l], blk + 1)
                act.wait_ge(o_out[l], 16 * (blk + 1))
                c0 = OUT_AT[0] if l == 0 else OUT_AT[1]
                c1 = OUT_AT[1] if l == 0 else OUT_COLS
                nc.scalar.activation(o_row[l][:, :], summed[0:BT, c0:c1], ACT.Copy).then_inc(o_in[l], 1)

            highs(0, 0, 0)
            highs(0, 0, 1)
            for l in (1, 2):
                for g in pieces(l):
                    a, n = piece(l, g)
                    at = slice(a - WHOLE_CHUNKS[l], a - WHOLE_CHUNKS[l] + n)
                    act.wait_ge(w_in[l][g], W_COUNT[g])
                    high_w(w_split[l][:, at, :], stage(l)[:, at, :])
            second_halves(0, 0)
            act.wait_ge(ones_hid, 2)
            hidden(0, 0)
            relu(0, 0)
            results(0, 0)
            for b in range(WHOLE[1], AHEAD):
                highs(1, 0, b)

            def step(n, more):
                for layer, blk, b in order(n, more):
                    if (layer, b) == (2, 0):
                        second_halves(1, n)
                        hidden(1, n)
                        relu(1, n)
                    if b >= WHOLE[layer]:
                        highs(layer, blk, b)
                    if more:
                        if (layer, b) == (2, 1):
                            second_halves(0, n + 1)
                        if (layer, b) == (2, 2):
                            relu(0, n + 1)
                        if (layer, b) == (2, 4):
                            hidden(0, n + 1)
                        if (layer, b) == (2, 5):
                            results(0, n + 1)
                        if (layer, b) == (1, 3):
                            second_halves(2, n)
                        if (layer, b) == (1, 4):
                            relu(2, n)
                        if (layer, b) == (1, 5):
                            results(2, n)
                if not more:
                    second_halves(2, n)
                    relu(2, n)
                    results(2, n)

            with act.Fori(0, BLOCKS - 1) as n:
                step(n, True)
            step(BLOCKS - 1, False)

        @block.tensor
        def _(pe):
            def multiply(layer, blk, b, between=None):
                c0, n = BATCHES[layer][b]
                is_whole = b < WHOLE[layer]
                chunks = L0_CHUNKS if layer == 0 else CHUNKS
                rows = L0_ROWS if layer == 0 else P
                k = b - WHOLE[layer]
                if is_whole:
                    pe.wait_ge(whole, whole_number(layer, blk, b) + 1)
                else:
                    pe.wait_ge(low, split_number(layer, blk, k) + 1)
                slot = None if is_whole else ring_slot(layer, blk, k)
                for c in range(c0, c0 + n):
                    if between and c == c0 + between[0]:
                        between[1]()
                    first, end = c == 0, c == chunks - 1
                    at = (c - c0) * T
                    for t in range(TILES):
                        a = acc[layer][t]
                        tok = slice(at + t * P, at + (t + 1) * P)
                        if is_whole:
                            last = nc.tensor.matmul(a[:, 0:O], z_whole[whole_number(layer, 0, b) % WHOLE_RING][:, tok], w_whole[layer][:, c, :], start=first, stop=False,
                                                    skip_group_check=True)
                        else:
                            w = w_split[layer][0:rows, c - WHOLE_CHUNKS[layer], :]
                            nc.tensor.matmul(a[:, 0:2 * O], z_high[slot][0:rows, tok], w, start=first, stop=False,
                                             skip_group_check=True)
                            last = nc.tensor.matmul(a[:, 0:O], z_low[slot][0:rows, tok], w[:, 0:O], start=False, stop=end,
                                                    skip_group_check=True)
                            if end and t == 0:
                                last.then_inc(tile0[layer], 1)
                last.then_inc(whole_used if is_whole else slots_freed, 1)

            def transpose(layer, blk):
                pe.wait_ge(s_in[layer], TILES * (blk + 1))
                tn = transpose_number(layer, blk)
                if layer == 1:
                    pe.wait_ge(hid_in[1], 3 * blk + 3)
                else:
                    pe.wait_ge(hid_in[2], 3 * blk)
                for t in range(TILES):
                    last = nc.tensor.transpose(turned[0:HID, t * P:(t + 1) * P], s[layer][:, t, 0:HID], ident[:, :])
                last.then_inc(turned_in, 1)

            def sum_over_d(layer, blk):
                pe.wait_ge(relu_done[layer], blk + 1)
                a, b = DIRECT[layer]
                at = OUT_AT[layer]
                for t in range(TILES):
                    last = nc.tensor.matmul(summed[0:BT, at:at + b - a], group_b[:, t, :], s[layer][:, t, a:b],
                                            start=(t == 0), stop=(t == TILES - 1), skip_group_check=True)
                last.then_inc(direct_summed[layer], 1)

            pe.wait_ge(w_low_done, 1)
            pe.wait_ge(consts, 2)
            multiply(0, 0, 0)
            multiply(0, 0, 1)
            transpose(0, 0)
            sum_over_d(0, 0)
            pe.wait_ge(w_low_done, piece_number(2, GROUPS - 1) + 1)
            pe.wait_ge(w_whole_in, 32 * sum(WHOLE[l] > 0 for l in WHOLE))

            for b in range(AHEAD):
                multiply(1, 0, b)

            def step(n, more):
                for layer, blk, b in order(n, more):
                    if not more and (layer, b) == (2, 0):
                        transpose(1, n)
                    multiply(layer, blk, b, (2, lambda: transpose(1, n)) if (layer, b) == (0, 0) else None)
                    if (layer, b) == (2, 0):
                        sum_over_d(1, n)
                    if more:
                        if (layer, b) == (2, 2):
                            transpose(0, n + 1)
                            sum_over_d(0, n + 1)
                        if (layer, b) == (1, 2):
                            sum_over_d(2, n)
                if not more:
                    sum_over_d(2, n)

            with pe.Fori(0, BLOCKS - 1) as n:
                step(n, True)
            step(BLOCKS - 1, False)


_INS = ["r_x", "L0_rec_W0", "L0_rec_W1", "L0_rec_W2", "L0_rec_b0", "L0_rec_b1", "L0_rec_b2"]
_OUTS = [((B, OUT_COLS), "float32")]


def kernel(**inputs):
    import numpy as _np
    import concourse.bacc as _bacc
    from concourse import mybir as _mybir
    from concourse.bass_utils import run_bass_kernel_spmd as _run

    nc = _bacc.Bacc("TRN2", target_bir_lowering=False, num_devices=1)
    arrays, args = {}, []
    for name in _INS:
        a = _np.ascontiguousarray(inputs[name])
        arrays[f"in_{name}_dram"] = a
        args.append(nc.dram_tensor(f"in_{name}_dram", a.shape, _mybir.dt.from_np(a.dtype), kind="ExternalInput").ap())
    for i, (shape, dtype) in enumerate(_OUTS):
        dt = _mybir.dt.from_np(_np.dtype(dtype))
        args.append(nc.dram_tensor(f"out_{i}_dram", shape, dt, kind="ExternalOutput").ap())
    cin_kernel(nc, *args)
    r = _run(nc, [arrays], core_ids=[0])
    return r.results[0]["out_0_dram"]
```
